# Optimizing a Trainium2 kernel written in Bass

```python
import numpy as np
import jax
import jax.numpy as jnp

def _softmax(x, axis=-1):
    return jax.nn.softmax(x, axis=axis)

def _gelu(x):
    return jax.nn.gelu(x, approximate=True)

def _silu(x):
    return jax.nn.silu(x)

def _sigmoid(x):
    return jax.nn.sigmoid(x)

def _layernorm(x, axis=-1, eps=1e-05):
    m = jnp.mean(x, axis=axis, keepdims=True)
    v = jnp.var(x, axis=axis, keepdims=True)
    return (x - m) / jnp.sqrt(v + eps)

def _scatter_add(tgt, idx, src, axis=0):
    return tgt.at[idx].add(src)

def _segment_sum(src, seg, n):
    return jax.ops.segment_sum(src, seg, n)
kernel_name = 'mk_xattn_seq_d1_seqx_r2_4e2fd5'

def setup_inputs(seed: int=0):
    np.random.seed(seed)
    _w = jnp.asarray

    def _rec_inputs():
        import jax
        import jax.numpy as jnp
        _rk = jax.random.key(seed)
        x = 7.22e-05 + 1 * jax.random.normal(jax.random.fold_in(_rk, 1), (32, 512, 512), jnp.float32)
        _lenS = 512 - jax.random.randint(jax.random.fold_in(_rk, 7), (32,), 0, max(1, 512 // 4) + 1, jnp.int32)
        _lenS2 = 512 - jax.random.randint(jax.random.fold_in(_rk, 8), (32,), 0, max(1, 512 // 4) + 1, jnp.int32)
        _ctx_1024P = jax.random.normal(jax.random.fold_in(_rk, 11), (32, 16, 512), jnp.float32)
        _ctx_1024c = jax.random.dirichlet(jax.random.fold_in(_rk, 511), 0.3 * jnp.ones((16,), jnp.float32), (32, 512))
        _ctx_1024t = jnp.einsum('bsk,bkd->bsd', _ctx_1024c, _ctx_1024P)
        _ctx_1024t = _ctx_1024t * jax.lax.rsqrt(jnp.mean(jnp.square(_ctx_1024t)) + 1e-12) * 0.953939
        ctx_1024 = 4.13588e-05 + 0.999923 * (_ctx_1024t + 0.3 * jax.random.normal(jax.random.fold_in(_rk, 611), (32, 512, 512), jnp.float32))
        return (x, ctx_1024)
    x, ctx_1024 = _rec_inputs()

    def _L0_xattn_setup():
        import jax, jax.numpy as jnp
        import numpy as np
        NH = 16
        key = jax.random.key(seed)
        ks = jax.random.split(key, 5)
        B, N, D = (4, 1024, 512)
        return {'tgt': jax.random.normal(ks[0], (B, N, D), dtype=jnp.float32), 'memory': jax.random.normal(ks[1], (B, N, D), dtype=jnp.float32), 'Wq': jax.random.normal(ks[2], (D, D), dtype=jnp.float32) * (1.0 / np.sqrt(D)), 'Wk': jax.random.normal(ks[3], (D, D), dtype=jnp.float32) * (1.0 / np.sqrt(D)), 'Wv': jax.random.normal(ks[4], (D, D), dtype=jnp.float32) * (1.0 / np.sqrt(D))}
    _L0_xattn_all = _L0_xattn_setup()
    _L0_xattn_in = {k: v for k, v in _L0_xattn_all.items() if k in ('Wq', 'Wk', 'Wv')}
    del _L0_xattn_all
    return {'x': x, 'ctx_1024': ctx_1024, 'L0_xattn_Wq': _L0_xattn_in['Wq'], 'L0_xattn_Wk': _L0_xattn_in['Wk'], 'L0_xattn_Wv': _L0_xattn_in['Wv']}

def reference(x, ctx_1024, L0_xattn_Wq, L0_xattn_Wk, L0_xattn_Wv):
    import jax
    import jax.numpy as jnp

    def _L0_xattn_ref(tgt, memory, Wq, Wk, Wv):
        import jax, jax.numpy as jnp
        import numpy as np
        NH = 16
        B, N, D = tgt.shape
        dk = D // NH
        scale = 1.0 / np.sqrt(dk)
        q = (tgt @ Wq.T).reshape(B, N, NH, dk).transpose(0, 2, 1, 3)
        k = (memory @ Wk.T).reshape(B, N, NH, dk).transpose(0, 2, 1, 3)
        v = (memory @ Wv.T).reshape(B, N, NH, dk).transpose(0, 2, 1, 3)
        scores = jnp.einsum('bhqd,bhkd->bhqk', q, k) * scale
        probs = jax.nn.softmax(scores, axis=-1)
        att = jnp.einsum('bhqk,bhkd->bhqd', probs, v)
        att = att.transpose(0, 2, 1, 3).reshape(B, N, D)
        tgt2 = att[0]
        return tgt + tgt2
    x = _L0_xattn_ref(x, ctx_1024, L0_xattn_Wq, L0_xattn_Wk, L0_xattn_Wv)
    return x

_drawn_inputs = setup_inputs


def setup_inputs(seed=0):
    import zlib

    import numpy as np

    out = dict(_drawn_inputs(seed))
    spreads = {}
    factors = {}
    for name, (base, spread) in spreads.items():
        noise = np.random.default_rng([zlib.crc32(name.encode()), seed]).standard_normal(out[name].shape)
        drawn = base * np.exp(spread * noise) if base else spread * noise
        out[name] = jnp.asarray(drawn.astype(out[name].dtype))
    for name, factor in factors.items():
        out[name] = (out[name] * factor).astype(out[name].dtype)
    return out
```

```python
from contextlib import ExitStack

import concourse.bass as bass
from concourse import mybir

F32 = mybir.dt.float32
ALU = mybir.AluOpType
ACT = mybir.ActivationFunctionType
AX_X = mybir.AxisListType.X

P = 128
HEADS = 16
DK = 32
HPG = P // DK
BPG = 4


def cross_attention_add(nc, x, ctx, wq, wk, wv, out):
    B, N, D = x.shape
    T = N // P
    C = D // P
    HG = HEADS // HPG
    G = B // BPG
    RING = G - 1
    AHEAD = 3
    S_BANKS = AHEAD + 1
    PT_SLOTS = HPG + 2
    SCALE = float(DK) ** -0.5
    DVE_GROUPS = (0, 1, 3, 4, 6)
    POOL_GROUPS = (2, 5, 7)
    assert T == 4 and C == 4 and HG == 4 and N == 512 and D == HEADS * DK

    x_rows = x.rearrange("b (j p) d -> p j b d", p=P)
    out_rows = out.rearrange("b (j p) d -> p j b d", p=P)

    with ExitStack() as stack:
        def sb(name, shape):
            return stack.enter_context(nc.sbuf_tensor(name, shape, F32))

        def sem(name):
            return stack.enter_context(nc.semaphore(name))

        x_first = sb("x_first", [P, T, BPG, D])
        ring = sb("ring", [P, 2 * RING, BPG, D])
        CTX_RAW, WK_RAW, WQ_RAW, WV_RAW, WK_T, WV_T, CTX_T = range(RING, 2 * RING)
        ctx_raw, wk_raw, wq_raw, wv_raw = (ring[:, s, :, :] for s in (CTX_RAW, WK_RAW, WQ_RAW, WV_RAW))
        wk_t, wv_t, ctx_t = (ring[:, s, :, :] for s in (WK_T, WV_T, CTX_T))

        ident = sb("ident", [P, P])
        x0_t = sb("x0_t", [P, C, N])
        wq_t = sb("wq_t", [P, C, D])
        k_t = sb("k_t", [P, HG, N])
        v = sb("v", [P, T, D])
        q_diag = sb("q_diag", [P, HEADS, P])
        probs = sb("probs", [P, 2, N])
        probs_t = sb("probs_t", [P, PT_SLOTS, T, P])
        att_t = sb("att_t", [P, HG, P])
        att = sb("att", [P, D])
        neg_max = sb("neg_max", [P, HEADS])
        row_sum = sb("row_sum", [P, HEADS])
        recip = sb("recip", [P, HEADS])
        q_diag_by_group = q_diag[:, :, :].rearrange("p (g h) n -> p g h n", h=HPG)

        bank = stack.enter_context(nc.psum_tensor("bank", [P, 8, 512], F32))
        PT_BANK, ATT_T_BANK, MISC_BANK = S_BANKS, S_BANKS + 2, S_BANKS + 3
        att_t_ps = bank[:, ATT_T_BANK, :].rearrange("p (g n) -> p g n", g=HG)
        misc_ps = bank[:, MISC_BANK, :].rearrange("p (g n) -> p g n", g=HG)

        ctx_loaded, wk_loaded, x0_loaded, wq_loaded, wv_loaded = (
            sem(n) for n in ("ctx_loaded", "wk_loaded", "x0_loaded", "wq_loaded", "wv_loaded"))
        loaded = [sem(f"loaded{g}") for g in range(G)]
        added = [sem(f"added{g}") for g in range(G)]
        stored = [sem(f"stored{g}") for g in range(G)]
        ident_ready, q_zeroed = sem("ident_ready"), sem("q_zeroed")
        bank_filled, dve_evacuated, act_evacuated = sem("bank_filled"), sem("dve_evacuated"), sem("act_evacuated")
        q_projected, q_ready = sem("q_projected"), sem("q_ready")
        scores_ready, max_ready, exp_ready = sem("scores_ready"), sem("max_ready"), sem("exp_ready")
        transposed, probs_t_ready = sem("transposed"), sem("probs_t_ready")
        att_t_summed, att_t_ready = sem("att_t_summed"), sem("att_t_ready")
        att_back, recip_ready, att_ready = sem("att_back"), sem("recip_ready"), sem("att_ready")

        def transposes(raw, to):
            return [("transpose", raw, to, c) for c in range(C)]

        jobs = (transposes(ctx_raw, ctx_t) + transposes(wk_raw, wk_t) + [("keys", None, k_t, g) for g in range(HG)]
                + transposes(x_first[:, :, 0, :], x0_t) + transposes(wq_raw, wq_t))
        Q_AT = len(jobs)
        jobs += transposes(wv_raw, wv_t) + [("values", None, v, t) for t in range(T)]
        JOBS = len(jobs)
        CTX_T_DONE, WK_T_DONE, K_DONE, X0_T_DONE, WQ_T_DONE, WV_T_DONE, V_DONE = range(4, 4 * 7 + 1, 4)
        job_bank = [n % 8 for n in range(Q_AT)] + [(n + PT_BANK) % MISC_BANK for n in range(JOBS - Q_AT)]

        def emptied(eng, n):
            eng.wait_ge(dve_evacuated, (n + 1) // 2)
            if n >= 2:
                eng.wait_ge(act_evacuated, n // 2)

        def job_out(n):
            _, _, to, i = jobs[n]
            return to[:, i, :], bank[:, job_bank[n], :]

        block = stack.enter_context(nc.Block())

        @block.sync
        def _(sp):
            def load(j, g, slot):
                if g == 0:
                    sp.dma_start(x_first[:, j, 1:BPG, :], x_rows[:, j, 1:BPG, :]).then_inc(loaded[0], 16)
                else:
                    sp.dma_start(ring[:, slot, :, :], x_rows[:, j, g * BPG:(g + 1) * BPG, :]).then_inc(loaded[g], 16)

            def store(j, g, slot):
                sp.wait_ge(added[g], j + 1)
                src = x_first[:, j, :, :] if g == 0 else ring[:, slot, :, :]
                sp.dma_start(out_rows[:, j, g * BPG:(g + 1) * BPG, :], src).then_inc(stored[g], 16)

            def reload(j, g):
                sp.wait_ge(stored[g], (j + 1) * 16)
                sp.wait_ge(loaded[g], (j + 2) * 16)
                load(j + 2, g, j * RING + g - 1)

            sp.dma_start(ctx_raw, ctx[0].rearrange("(t p) d -> p t d", p=P)).then_inc(ctx_loaded, 16)
            sp.dma_start(wk_raw, wk.rearrange("(t p) d -> p t d", p=P)).then_inc(wk_loaded, 16)
            sp.dma_start(x_first[:, :, 0, :], x_rows[:, :, 0, :]).then_inc(x0_loaded, 16)
            sp.dma_start(wq_raw, wq.rearrange("(t p) d -> p t d", p=P)).then_inc(wq_loaded, 16)
            sp.dma_start(wv_raw, wv.rearrange("(t p) d -> p t d", p=P)).then_inc(wv_loaded, 16)
            for g in range(G):
                load(0, g, g - 1)
            held_until = {CTX_RAW: CTX_T_DONE, WK_RAW: WK_T_DONE, WQ_RAW: WQ_T_DONE, WV_RAW: WV_T_DONE,
                          WK_T: K_DONE, WV_T: V_DONE, CTX_T: V_DONE}
            for g in range(G):
                slot = RING + g - 1
                if g > 0:
                    sp.wait_ge(bank_filled, held_until[slot])
                sp.wait_ge(loaded[g], 16)
                load(1, g, slot)
            for j in (2, 3):
                sp.wait_ge(loaded[0], j * 16)
                load(j, 0, None)
            LAG = 2
            with sp.Fori(0, 2) as j:
                for g in range(G):
                    store(j, g, j * RING + g - 1)
                    if g - LAG >= 1:
                        reload(j, g - LAG)
                for g in range(G - LAG, G):
                    reload(j, g)
            with sp.Fori(0, 2) as k:
                for g in range(G):
                    store(k + 2, g, k * RING + g - 1)
            for g in range(G):
                sp.wait_ge(stored[g], T * 16)

        @block.gpsimd
        def _(pool):
            nc.gpsimd.memset(ident[:, :], 0.0).then_inc(ident_ready, 1)
            pool.wait_ge(ident_ready, 1)
            nc.gpsimd.affine_select(out=ident[:, :], in_=ident[:, :], compare_op=ALU.not_equal, fill=1.0, base=0,
                                    pattern=[[-1, P]], channel_multiplier=1).then_inc(ident_ready, 1)
            nc.gpsimd.memset(q_diag[:, :, :], 0.0).then_inc(q_zeroed, 1)
            with pool.Fori(0, T) as j:
                pool.wait_ge(att_ready, j + 1)
                for g in POOL_GROUPS:
                    pool.wait_ge(loaded[g], (j + 1) * 16)
                    xs = ring[:, (j % 2) * RING + (g - 1), :, :]
                    nc.gpsimd.tensor_tensor(xs, xs, att[:, :].unsqueeze(1).to_broadcast([P, BPG, D]),
                                            ALU.add).then_inc(added[g], 1)

        @block.tensor
        def _(pe):
            mm = nc.tensor.matmul
            inputs = {0: ctx_loaded, 4: wk_loaded, 12: x0_loaded, 16: wq_loaded, 20: wv_loaded}
            needs = {8: WK_T_DONE, 24: WV_T_DONE}

            def project_queries(j):
                for g in range(HG):
                    for c in range(C):
                        last = mm(misc_ps[:, g, :], wq_t[:, c, g * P:(g + 1) * P], x0_t[:, c, bass.ds(j * P, P)],
                                  start=(c == 0), stop=(c == C - 1))
                last.then_inc(q_projected, 1)

            pe.wait_ge(ident_ready, 2)
            used = {}
            for n, (kind, raw, to, i) in enumerate(jobs):
                if n == Q_AT:
                    emptied(pe, Q_AT)
                    project_queries(0)
                if n in inputs:
                    pe.wait_ge(inputs[n], 16)
                if n in needs:
                    emptied(pe, needs[n])
                b = job_bank[n]
                if b in used:
                    emptied(pe, used[b] + 1)
                used[b] = n
                for t in range(T):
                    if kind == "transpose":
                        last = nc.tensor.transpose(bank[:, b, t * P:(t + 1) * P], raw[:, t, i * P:(i + 1) * P], ident[:, :])
                    elif kind == "keys":
                        last = mm(bank[:, b, :], wk_t[:, t, i * P:(i + 1) * P], ctx_t[:, t, :],
                                  start=(t == 0), stop=(t == C - 1))
                    else:
                        last = mm(bank[:, b, :], ctx_t[:, t, i * P:(i + 1) * P], wv_t[:, t, :],
                                  start=(t == 0), stop=(t == C - 1))
                last.then_inc(bank_filled, 1)

            def scores(j, h):
                if h % (HEADS // 2) == 0:
                    pe.wait_ge(q_ready, 2 * j + 1 + h // (HEADS // 2))
                mm(bank[:, h % S_BANKS, :], q_diag[:, h, :], k_t[:, h // HPG, :], start=True, stop=True
                   ).then_inc(scores_ready, 1)

            def values(j, g):
                pe.wait_ge(probs_t_ready, j * HEADS + (g + 1) * HPG)
                if not (isinstance(j, int) and j == 0 and g == 0):
                    pe.wait_ge(att_t_ready, j * HG + g)
                for t in range(T):
                    for i in range(HPG):
                        h = g * HPG + i
                        last = mm(att_t_ps[i * DK:(i + 1) * DK, g, :], v[:, t, h * DK:(h + 1) * DK],
                                  probs_t[:, h % PT_SLOTS, t, :], start=(t == 0), stop=(t == T - 1),
                                  tile_position=(0, i * DK))
                last.then_inc(att_t_summed, 1)

            def tile(j, more):
                for h in range(HEADS):
                    pe.wait_ge(exp_ready, j * HEADS + h + 1)
                    for t in range(T):
                        last = nc.tensor.transpose(bank[:, PT_BANK + h % 2, t * P:(t + 1) * P],
                                                   probs[:, h % 2, t * P:(t + 1) * P], ident[:, :])
                    last.then_inc(transposed, 1)
                    if h + AHEAD < HEADS:
                        scores(j, h + AHEAD)
                    elif more:
                        scores(j + 1, h + AHEAD - HEADS)
                    if h % HPG == 1 and h > HPG:
                        values(j, h // HPG - 1)
                    if h == HEADS // 2 and more:
                        if not (isinstance(j, int) and j == 0):
                            pe.wait_ge(att_ready, j)
                        project_queries(j + 1)
                values(j, HG - 1)
                pe.wait_ge(att_t_ready, (j + 1) * HG)
                if more:
                    pe.wait_ge(q_ready, 2 * j + 4)
                for g in range(HG):
                    last = nc.tensor.transpose(misc_ps[:, g, :], att_t[:, g, :], ident[:, :])
                last.then_inc(att_back, 1)

            emptied(pe, JOBS)
            for h in range(AHEAD):
                scores(0, h)
            tile(0, True)
            with pe.Fori(1, T - 1) as j:
                tile(j, True)
            tile(T - 1, False)

        @block.scalar
        def _(act):
            def spread_queries(half):
                gs = slice(half * HG // 2, (half + 1) * HG // 2)
                for i in range(HPG):
                    rows = slice(i * DK, (i + 1) * DK)
                    last = nc.scalar.mul(q_diag_by_group[rows, gs, i, :], misc_ps[rows, gs, :], SCALE)
                last.then_inc(q_ready, 1)

            def empty(n):
                act.wait_ge(bank_filled, n + 1)
                to, ps = job_out(n)
                nc.scalar.copy(to, ps).then_inc(act_evacuated, 1)

            for n in range(1, Q_AT, 2):
                empty(n)
            act.wait_ge(q_zeroed, 1)
            act.wait_ge(q_projected, 1)
            for half in range(2):
                spread_queries(half)
            for n in range(Q_AT + 1, JOBS, 2):
                empty(n)

            def copy_transposed(j, h):
                act.wait_ge(transposed, j * HEADS + h + 1)
                nc.scalar.copy(probs_t[:, h % PT_SLOTS, :, :],
                               bank[:, PT_BANK + h % 2, :].rearrange("p (t n) -> p t n", t=T)).then_inc(probs_t_ready, 1)

            def tile(j, more):
                for h in range(HEADS):
                    act.wait_ge(max_ready, j * HEADS + h + 1)
                    nc.scalar.activation(probs[:, h % 2, :], bank[:, h % S_BANKS, :], ACT.Exp, bias=neg_max[:, h:h + 1],
                                         scale=1.0, accum_out=row_sum[:, h:h + 1]).then_inc(exp_ready, 1)
                    if h >= 1:
                        copy_transposed(j, h - 1)
                    if more and h == HEADS // 2 + 2:
                        act.wait_ge(q_projected, j + 2)
                        act.wait_ge(scores_ready, j * HEADS + HEADS // 2)
                        spread_queries(0)
                if more:
                    act.wait_ge(scores_ready, (j + 1) * HEADS)
                    spread_queries(1)
                copy_transposed(j, HEADS - 1)

            tile(0, True)
            with act.Fori(1, T - 1) as j:
                tile(j, True)
            tile(T - 1, False)

        @block.vector
        def _(dve):
            for n in range(0, JOBS, 2):
                dve.wait_ge(bank_filled, n + 1)
                to, ps = job_out(n)
                nc.vector.tensor_copy(to, ps).then_inc(dve_evacuated, 1)

            def head_max(j, h):
                dve.wait_ge(scores_ready, j * HEADS + h + 1)
                nc.vector.tensor_reduce(neg_max[:, h:h + 1], bank[:, h % S_BANKS, :], AX_X, ALU.max,
                                        negate=True).then_inc(max_ready, 1)

            def invert_sums(j, g):
                dve.wait_ge(exp_ready, j * HEADS + (g + 1) * HPG)
                cols = slice(g * HPG, (g + 1) * HPG)
                nc.vector.reciprocal(recip[:, cols], row_sum[:, cols]).then_inc(recip_ready, 1)

            def copy_att_t(j, g):
                dve.wait_ge(att_t_summed, j * HG + g + 1)
                nc.vector.tensor_copy(att_t[:, g, :], att_t_ps[:, g, :]).then_inc(att_t_ready, 1)

            def add(j, g):
                dve.wait_ge(att_ready, j + 1)
                if g == 0:
                    xs = x_first[:, j, :, :]
                else:
                    xs = ring[:, (j % 2) * RING + (g - 1), :, :]
                dve.wait_ge(loaded[g], (j + 1) * 16)
                nc.vector.tensor_tensor(xs, xs, att[:, :].unsqueeze(1).to_broadcast([P, BPG, D]),
                                        ALU.add).then_inc(added[g], 1)

            def tile(j, first, more):
                todo = [] if first else list(DVE_GROUPS)
                for h in range(2, HEADS):
                    head_max(j, h)
                    if h % HPG == 2 and h > HPG:
                        invert_sums(j, h // HPG - 1)
                    if h % HPG == 0 and h > HPG:
                        copy_att_t(j, h // HPG - 2)
                    if todo and h % 2:
                        add(j - 1, todo.pop(0))
                invert_sums(j, HG - 1)
                copy_att_t(j, HG - 2)
                if more:
                    for h in range(2):
                        head_max(j + 1, h)
                copy_att_t(j, HG - 1)
                dve.wait_ge(att_back, j + 1)
                dve.wait_ge(recip_ready, (j + 1) * HG)
                if not first:
                    for g in DVE_GROUPS + POOL_GROUPS:
                        dve.wait_ge(added[g], j)
                nc.vector.tensor_tensor(att[:, :].rearrange("p (h d) -> p h d", d=DK),
                                        bank[:, MISC_BANK, :].rearrange("p (h d) -> p h d", d=DK),
                                        recip[:, :].unsqueeze(2).to_broadcast([P, HEADS, DK]),
                                        ALU.mult).then_inc(att_ready, 1)

            for h in range(2):
                head_max(0, h)
            tile(0, True, True)
            with dve.Fori(1, T - 1) as j:
                tile(j, False, True)
            tile(T - 1, False, False)
            for g in DVE_GROUPS:
                add(T - 1, g)


_INS = ["x", "ctx_1024", "L0_xattn_Wq", "L0_xattn_Wk", "L0_xattn_Wv"]


def kernel(**inputs):
    import numpy as _np
    import concourse.bacc as _bacc
    from concourse import mybir as _mybir
    from concourse.bass_utils import run_bass_kernel_spmd as _run

    nc = _bacc.Bacc("TRN2", target_bir_lowering=False, num_devices=1)
    arrays, args = {}, []
    for name in _INS:
        a = _np.ascontiguousarray(inputs[name])
        arrays[f"in_{name}_dram"] = a
        args.append(nc.dram_tensor(f"in_{name}_dram", a.shape, _mybir.dt.from_np(a.dtype), kind="ExternalInput").ap())
    shape = arrays["in_x_dram"].shape
    out = nc.dram_tensor("out_0_dram", shape, _mybir.dt.float32, kind="ExternalOutput").ap()
    cross_attention_add(nc, *args, out)
    r = _run(nc, [arrays], core_ids=[0])
    return r.results[0]["out_0_dram"]
```

```python
from contextlib import ExitStack

import concourse.bass as bass
from concourse import mybir

F32 = mybir.dt.float32
F32R = mybir.dt.float32r
ALU = mybir.AluOpType
ACT = mybir.ActivationFunctionType
AX_X = mybir.AxisListType.X

P = 128
HEADS = 16
DK = 32
HPG = P // DK
BPG = 4


def cross_attention_add(nc, x, ctx, wq, wk, wv, out):
    B, N, D = x.shape
    T = N // P
    C = D // P
    HG = HEADS // HPG
    G = B // BPG
    RING = G - 1
    HALF = D // 2
    HALF_HEADS, HALF_GROUPS = HEADS // 2, HG // 2
    AHEAD = 3
    MAX_AHEAD = 2
    S_BANKS = AHEAD + 1
    FIRST_BACK = 1
    PT_SLOTS = HPG + 2
    Q_SLOTS = 2 * HPG
    WARM_UP = 13
    SCALE = float(DK) ** -0.5
    HI, LO = 0, 1
    PASSES = ((HI, HI), (HI, LO), (LO, HI))
    DVE_GROUPS = (0, 2, 4)
    POOL_GROUPS = (1, 3, 5, 6, 7)
    assert T == 4 and C == 4 and HG == 4 and N == 512 and D == HEADS * DK

    x_rows = x.rearrange("b (j p) d -> p j b d", p=P)
    out_rows = out.rearrange("b (j p) d -> p j b d", p=P)

    with ExitStack() as stack:
        def sb(name, shape, dtype=F32, where=stack):
            return where.enter_context(nc.sbuf_tensor(name, shape, dtype))

        def sem(name):
            return stack.enter_context(nc.semaphore(name))

        x_first = sb("x_first", [P, T, BPG, D])
        CTX_RAW, WV_RAW, X0_T, WK_T, W_T, CTX_T = RING - 3, RING - 2, RING - 1, RING + 1, RING + 3, RING + 5
        with ExitStack() as early:
            sb("x_slots", [P, X0_T, BPG, D], where=early)
            x0_t = sb("x0_t", [P, 2, C, N], F32R, where=early)
            wk_t = sb("wk_t", [P, 2, C, D], F32R, where=early)
            w_t = sb("w_t", [P, 2, C, D], F32R, where=early)
            ctx_t = sb("ctx_t", [P, 2, C, N], F32R, where=early)
            wq_raw = sb("wq_raw", [P, C, D], where=early)
            wk_raw = sb("wk_raw", [P, C, D], where=early)
        ring = sb("ring", [P, 2 * RING, BPG, D])
        probs = sb("probs", [P, 2, N])
        probs_t = sb("probs_t", [P, PT_SLOTS, T, P])
        ctx_raw, wv_raw = ring[:, CTX_RAW, :, :], ring[:, WV_RAW, :, :]

        ident = sb("ident", [P, P])
        q_t = sb("q_t", [P, HG, N])
        q_diag = sb("q_diag", [P, 2, Q_SLOTS, P], F32R)
        k_t = sb("k_t", [P, 2, HG, N], F32R)
        v = sb("v", [P, T, D])
        att_t = sb("att_t", [P, HG, P])
        att = sb("att", [P, D])
        neg_max = sb("neg_max", [P, HEADS])
        row_sum = sb("row_sum", [P, HEADS])
        recip = sb("recip", [P, HEADS])

        bank = stack.enter_context(nc.psum_tensor("bank", [P, 8, 512], F32))
        PT_BANK, ATT_T_BANK, ATT_BANK = S_BANKS, S_BANKS + 2, S_BANKS + 3
        att_t_ps = bank[:, ATT_T_BANK, :].rearrange("p (g n) -> p g n", g=HG)
        att_ps = bank[:, ATT_BANK, :]

        ctx_loaded, wk_loaded, x0_loaded, wq_loaded, wv_loaded = (
            sem(n) for n in ("ctx_loaded", "wk_loaded", "x0_left_loaded", "wq_first_loaded", "wv_loaded"))
        wq_rest_loaded, x0_right_loaded = sem("wq_rest_loaded"), sem("x0_right_loaded")
        first_loaded, first_rest_loaded = sem("first_loaded"), sem("first_rest_loaded")
        loaded = [None] + [sem(f"loaded{g}") for g in range(1, G)]
        added = [sem(f"added{g}") for g in range(G)]
        stored = [sem(f"stored{g}") for g in range(G)]
        ident_ready, q_zeroed = sem("ident_ready"), sem("q_zeroed")
        bank_filled, dve_evacuated, act_evacuated = sem("bank_filled"), sem("dve_evacuated"), sem("act_evacuated")
        q_hi_ready, q_lo_ready = sem("q_hi_ready"), sem("q_lo_ready")
        scores_ready, max_ready, exp_ready = sem("scores_ready"), sem("max_ready"), sem("exp_ready")
        transposed, probs_t_ready = sem("transposed"), sem("probs_t_ready")
        att_t_summed, att_t_ready = sem("att_t_summed"), sem("att_t_ready")
        att_back, recip_ready, att_ready, att_ps_ready = (
            sem("att_back"), sem("recip_ready"), sem("att_ready"), sem("att_ps_ready"))

        STEPS = (["warm up", "wq_t", "wq_t", "x0_t", "x0_t", "x0_t", "x0_t", "queries", "wq_t", "queries", "wq_t"]
                 + ["wk_t", "wk_t", "queries", "wk_t", "wk_t", "ctx_t", "queries", "ctx_t", "ctx_t", "ctx_t"]
                 + ["keys", "wv_t", "wv_t", "keys", "wv_t", "wv_t", "keys", "lay out queries", "keys"]
                 + ["values", "values", "first scores", "values", "values"])
        VALUES_BANK = S_BANKS
        EVACUATION = {"queries": "act", "values": "dve"}
        jobs, job_bank, jobs_of, steps = [], [], {}, []
        for what in STEPS:
            if what in ("warm up", "lay out queries", "first scores"):
                steps.append(what)
            else:
                i = len(jobs_of.setdefault(what, []))
                jobs_of[what].append(len(jobs))
                steps.append(len(jobs))
                job_bank.append(VALUES_BANK + i if what == "values" else len(jobs) % 8)
                jobs.append((what, i, EVACUATION.get(what, "split")))
        last_job = {what: numbers[-1] + 1 for what, numbers in jobs_of.items()}
        OPERANDS = {"queries": ("x0_t", "wq_t"), "keys": ("ctx_t", "wk_t"), "values": ("ctx_t", "wv_t")}
        by_act = [how in ("split", "act") for *_, how in jobs]
        by_dve = [how in ("split", "dve") for *_, how in jobs]

        def emptied(eng, n):
            eng.wait_ge(act_evacuated, sum(by_act[:n]))
            eng.wait_ge(dve_evacuated, sum(by_dve[:n]))

        def job_dest(n):
            kind, i, how = jobs[n]
            if how == "split":
                to = {"wq_t": w_t, "x0_t": x0_t, "wk_t": wk_t, "ctx_t": ctx_t, "wv_t": w_t, "keys": k_t}[kind]
                if kind in ("wq_t", "wk_t"):
                    return to[:, HI, :, i * P:(i + 1) * P], to[:, LO, :, i * P:(i + 1) * P]
                return to[:, HI, i, :], to[:, LO, i, :]
            return q_t[:, i, :] if kind == "queries" else v[:, i, :]

        def as_dest(ps, dest):
            return ps.rearrange("p (c n) -> p c n", n=P) if len(dest.shape) == 3 else ps

        def unit(j, half=1):
            return j + half

        def unit_cols(j, half):
            return slice(half * HALF, (half + 1) * HALF) if isinstance(j, int) and j == 0 else slice(0, D)

        def x_slot(j, g, cols=slice(0, D)):
            if g == 0:
                return x_first[:, j, :, cols]
            return ring[:, (j % 2) * RING + (g - 1), :, cols]

        def laid_out_at(more):
            return [h for h in range(HPG // 2, HEADS, HPG) if h + Q_SLOTS < HEADS or more]

        block = stack.enter_context(nc.Block())

        @block.sync
        def _(sp):
            def load(j, g):
                sp.dma_start(x_slot(j, g), x_rows[:, j, g * BPG:(g + 1) * BPG, :]).then_inc(loaded[g], 16)

            def store(j, g, half=1):
                sp.wait_ge(added[g], unit(j, half) + 1)
                cols = unit_cols(j, half)
                sp.dma_start(out_rows[:, j, g * BPG:(g + 1) * BPG, cols], x_slot(j, g, cols)).then_inc(stored[g], 16)

            def reload(j, g):
                sp.wait_ge(stored[g], (unit(j) + 1) * 16)
                sp.wait_ge(loaded[g], (j + 2) * 16)
                load(j + 2, g)

            wq_rows = wq.rearrange("(t p) d -> p t d", p=P)
            sp.dma_start(wq_raw[:, 0:2, :], wq_rows[:, 0:2, :]).then_inc(wq_loaded, 16)
            for cols, loads in ((slice(0, HALF), x0_loaded), (slice(HALF, D), x0_right_loaded)):
                sp.dma_start(x_first[:, :, 0, cols], x_rows[:, :, 0, cols]).then_inc(loads, 16)
            sp.dma_start(wq_raw[:, 2:, :], wq_rows[:, 2:, :]).then_inc(wq_rest_loaded, 16)
            for rows, to, loads in ((wk, wk_raw, wk_loaded), (ctx[0], ctx_raw, ctx_loaded), (wv, wv_raw, wv_loaded)):
                sp.dma_start(to[:, :, :], rows.rearrange("(t p) d -> p t d", p=P)).then_inc(loads, 16)
            held_until = {CTX_RAW: last_job["ctx_t"], WV_RAW: last_job["wv_t"], X0_T: last_job["queries"],
                          X0_T + 1: last_job["queries"], WK_T: last_job["keys"], WK_T + 1: last_job["keys"]}
            sp.dma_start(x_first[:, 0, 1:BPG, :], x_rows[:, 0, 1:BPG, :]).then_inc(first_loaded, 16)
            for g in range(1, CTX_RAW + 1):
                load(0, g)
            for j in range(1, T):
                sp.dma_start(x_first[:, j, 1:BPG, :], x_rows[:, j, 1:BPG, :]).then_inc(first_rest_loaded, 16)
            for g in range(CTX_RAW + 1, G):
                sp.wait_ge(bank_filled, held_until[g - 1])
                load(0, g)
            for g in range(1, G):
                sp.wait_ge(bank_filled, held_until.get(RING + g - 1, len(jobs)))
                sp.wait_ge(loaded[g], 16)
                load(1, g)
            for g in range(G):
                store(0, g, 0)
            LAG = 2
            for j in range(2):
                for g in range(G):
                    store(j, g)
                    if g - LAG >= 1:
                        reload(j, g - LAG)
                for g in range(G - LAG, G):
                    reload(j, g)
            with sp.Fori(2, T) as j:
                for g in range(G):
                    store(j, g)
            for g in range(G):
                sp.wait_ge(stored[g], (unit(T - 1) + 1) * 16)

        @block.gpsimd
        def _(pool):
            nc.gpsimd.memset(ident[:, :], 0.0).then_inc(ident_ready, 1)
            pool.wait_ge(ident_ready, 1)
            nc.gpsimd.affine_select(out=ident[:, :], in_=ident[:, :], compare_op=ALU.not_equal, fill=1.0, base=0,
                                    pattern=[[-1, P]], channel_multiplier=1).then_inc(ident_ready, 1)

            nc.gpsimd.memset(q_diag[:, :, :, :].bitcast(F32), 0.0).then_inc(q_zeroed, 1)

            def add_unit(j, half=1):
                cols = unit_cols(j, half)
                pool.wait_ge(att_ready, unit(j, half) + 1)
                for g in POOL_GROUPS:
                    pool.wait_ge(loaded[g], (j + 1) * 16)
                    xs = x_slot(j, g, cols)
                    a = att[:, cols]
                    nc.gpsimd.tensor_tensor(xs, xs, a.unsqueeze(1).to_broadcast([P, BPG, a.shape[1]]),
                                            ALU.add).then_inc(added[g], 1)

            add_unit(0, 0)
            add_unit(0, 1)
            with pool.Fori(1, T) as j:
                add_unit(j)

        @block.tensor
        def _(pe):
            mm = nc.tensor.matmul
            inputs = {("wq_t", 0): wq_loaded, ("wq_t", 2): wq_rest_loaded, ("x0_t", 0): x0_loaded,
                      ("x0_t", C // 2): x0_right_loaded, ("wk_t", 0): wk_loaded, ("ctx_t", 0): ctx_loaded,
                      ("wv_t", 0): wv_loaded}
            raws = {"wq_t": wq_raw, "x0_t": x_first[:, :, 0, :], "wk_t": wk_raw, "ctx_t": ctx_raw, "wv_t": wv_raw}

            def project(n):
                kind, i, _ = jobs[n]
                ps = bank[:, job_bank[n], :]
                if (kind, i) in inputs:
                    pe.wait_ge(inputs[kind, i], 16)
                users = [m + 1 for m in range(n) if job_bank[m] == job_bank[n]]
                if users:
                    emptied(pe, users[-1])
                if kind in raws:
                    for m in range(T):
                        t, c = (i, m) if kind in ("wq_t", "wk_t") else (m, i)
                        last = nc.tensor.transpose(ps[:, m * P:(m + 1) * P], raws[kind][:, t, c * P:(c + 1) * P], ident[:, :])
                else:
                    chunk = slice(i * P, (i + 1) * P)
                    for c in range(C):
                        a_job, b_job = (jobs_of[operand] for operand in OPERANDS[kind])
                        b_job = b_job[c if kind == "values" else i]
                        if i == 0 or c == 0:
                            emptied(pe, max(a_job[c], b_job) + 1)
                        for a, b in PASSES:
                            left, right = {"queries": (w_t[:, a, c, chunk], x0_t[:, b, c, :]),
                                           "keys": (wk_t[:, a, c, chunk], ctx_t[:, b, c, :]),
                                           "values": (ctx_t[:, a, c, chunk], w_t[:, b, c, :])}[kind]
                            last = mm(ps, left, right,
                                      start=(c == 0 and (a, b) == PASSES[0]), stop=(c == C - 1 and (a, b) == PASSES[-1]))
                last.then_inc(bank_filled, 1)

            def scores(j, h):
                g = h // HPG
                if h % HPG == 0:
                    pe.wait_ge(q_lo_ready, j * HG + g + 1)
                for a, b in PASSES:
                    last = mm(bank[:, h % S_BANKS, :], q_diag[:, a, h % Q_SLOTS, :], k_t[:, b, g, :],
                              start=((a, b) == PASSES[0]), stop=((a, b) == PASSES[-1]))
                last.then_inc(scores_ready, 1)

            def weigh_values(j, g):
                pe.wait_ge(probs_t_ready, j * HEADS + (g + 1) * HPG)
                if isinstance(j, int) and j == 0 and g == 0:
                    emptied(pe, len(jobs))
                else:
                    pe.wait_ge(att_t_ready, j * HG + g)
                for t in range(T):
                    for i in range(HPG):
                        h = g * HPG + i
                        last = mm(att_t_ps[i * DK:(i + 1) * DK, g, :], v[:, t, h * DK:(h + 1) * DK],
                                  probs_t[:, h % PT_SLOTS, t, :], start=(t == 0), stop=(t == T - 1),
                                  tile_position=(0, i * DK))
                last.then_inc(att_t_summed, 1)

            def turn_back(j, groups, half=1):
                pe.wait_ge(att_t_ready, j * HG + groups.stop)
                if not (isinstance(j, int) and unit(j, half) == 0):
                    pe.wait_ge(added[DVE_GROUPS[-1]], unit(j, half))
                for g in groups:
                    last = nc.tensor.transpose(att_ps[:, g * P:(g + 1) * P], att_t[:, g, :], ident[:, :])
                last.then_inc(att_back, 1)

            def heads(j, more):
                for h in range(HEADS):
                    pe.wait_ge(exp_ready, j * HEADS + h + 1)
                    for t in range(T):
                        last = nc.tensor.transpose(bank[:, PT_BANK + h % 2, t * P:(t + 1) * P],
                                                   probs[:, h % 2, t * P:(t + 1) * P], ident[:, :])
                    last.then_inc(transposed, 1)
                    if isinstance(j, int) and j == 0 and h == HALF_HEADS + FIRST_BACK:
                        turn_back(0, range(0, HALF_GROUPS), 0)
                    if h + AHEAD < HEADS:
                        scores(j, h + AHEAD)
                    elif more:
                        scores(j + 1, h + AHEAD - HEADS)
                    if h % HPG == 0 and h > 0:
                        weigh_values(j, h // HPG - 1)
                weigh_values(j, HG - 1)

            pe.wait_ge(ident_ready, 2)
            for what in steps:
                if what == "warm up":
                    for _ in range(WARM_UP):
                        nc.tensor.transpose(bank[:, 7, 0:P], ident[:, :], ident[:, :])
                elif what == "first scores":
                    emptied(pe, last_job["keys"])
                    for h in range(AHEAD):
                        scores(0, h)
                elif isinstance(what, int):
                    project(what)
            emptied(pe, jobs_of["values"][1] + 1)
            heads(0, True)
            turn_back(0, range(HALF_GROUPS, HG))
            with pe.Fori(1, T - 1) as j:
                heads(j, True)
                turn_back(j, range(HG))
            heads(T - 1, False)
            turn_back(T - 1, range(HG))

        @block.scalar
        def _(act):
            def empty(n):
                if by_act[n]:
                    act.wait_ge(bank_filled, n + 1)
                    ps = bank[:, job_bank[n], :]
                    if jobs[n][0] == "queries":
                        nc.scalar.mul(job_dest(n), ps, SCALE).then_inc(act_evacuated, 1)
                    else:
                        high, _ = job_dest(n)
                        nc.scalar.copy(high, as_dest(ps, high)).then_inc(act_evacuated, 1)

            def query_high(j, g):
                for i in range(HPG):
                    rows = slice(i * DK, (i + 1) * DK)
                    last = nc.scalar.copy(q_diag[rows, HI, (g * HPG + i) % Q_SLOTS, :], q_t[rows, g, bass.ds(j * P, P)])
                last.then_inc(q_hi_ready, 1)

            def copy_transposed(j, h):
                act.wait_ge(transposed, j * HEADS + h + 1)
                nc.scalar.copy(probs_t[:, h % PT_SLOTS, :, :],
                               bank[:, PT_BANK + h % 2, :].rearrange("p (t n) -> p t n", t=T)).then_inc(probs_t_ready, 1)

            def heads(j, more):
                for h in range(HEADS):
                    act.wait_ge(max_ready, j * HEADS + h + 1)
                    nc.scalar.activation(probs[:, h % 2, :], bank[:, h % S_BANKS, :], ACT.Exp, bias=neg_max[:, h:h + 1],
                                         scale=1.0, accum_out=row_sum[:, h:h + 1]).then_inc(exp_ready, 1)
                    if h > 0:
                        copy_transposed(j, h - 1)
                    if h in laid_out_at(more):
                        g = (h + Q_SLOTS) // HPG
                        act.wait_ge(scores_ready, j * HEADS + (g - 1) * HPG)
                        query_high(j + g // HG, g % HG)
                copy_transposed(j, HEADS - 1)

            for what in steps:
                if what == "lay out queries":
                    act.wait_ge(q_zeroed, 1)
                    act.wait_ge(act_evacuated, sum(by_act[:last_job["queries"]]))
                    for g in range(Q_SLOTS // HPG):
                        query_high(0, g)
                elif isinstance(what, int):
                    empty(what)
            with act.Fori(0, T - 1) as j:
                heads(j, True)
            heads(T - 1, False)

        @block.vector
        def _(dve):
            def empty(n):
                if by_dve[n]:
                    ps = bank[:, job_bank[n], :]
                    if jobs[n][-1] == "split":
                        high, low = job_dest(n)
                        dve.wait_ge(act_evacuated, sum(by_act[:n + 1]))
                        nc.vector.tensor_tensor(low, as_dest(ps, low), high.bitcast(F32),
                                                ALU.subtract).then_inc(dve_evacuated, 1)
                    else:
                        dve.wait_ge(bank_filled, n + 1)
                        nc.vector.tensor_copy(job_dest(n), ps).then_inc(dve_evacuated, 1)

            def query_low(j, g):
                dve.wait_ge(q_hi_ready, j * HG + g + 1)
                for i in range(HPG):
                    rows, slot = slice(i * DK, (i + 1) * DK), (g * HPG + i) % Q_SLOTS
                    last = nc.vector.tensor_tensor(q_diag[rows, LO, slot, :], q_t[rows, g, bass.ds(j * P, P)],
                                                   q_diag[rows, HI, slot, :].bitcast(F32), ALU.subtract)
                last.then_inc(q_lo_ready, 1)

            def head_max(j, h):
                dve.wait_ge(scores_ready, j * HEADS + h + 1)
                nc.vector.tensor_reduce(neg_max[:, h:h + 1], bank[:, h % S_BANKS, :], AX_X, ALU.max,
                                        negate=True).then_inc(max_ready, 1)

            def invert_sums(j, g):
                dve.wait_ge(exp_ready, j * HEADS + (g + 1) * HPG)
                cols = slice(g * HPG, (g + 1) * HPG)
                nc.vector.reciprocal(recip[:, cols], row_sum[:, cols]).then_inc(recip_ready, 1)

            def copy_att_t(j, g):
                dve.wait_ge(att_t_summed, j * HG + g + 1)
                nc.vector.tensor_copy(att_t[:, g, :], att_t_ps[:, g, :]).then_inc(att_t_ready, 1)

            def normalize(j, half=1):
                cols = unit_cols(j, half)
                hs = slice(cols.start // DK, cols.stop // DK)
                dve.wait_ge(att_back, unit(j, half) + 1)
                dve.wait_ge(recip_ready, j * HG + hs.stop // HPG)
                if j > 0:
                    dve.wait_ge(added[POOL_GROUPS[-1]], unit(j, half))
                back = att_ps[:, cols].rearrange("p (h d) -> p h d", d=DK)
                inverse = recip[:, hs].unsqueeze(2).to_broadcast([P, hs.stop - hs.start, DK])
                nc.vector.tensor_tensor(att[:, cols].rearrange("p (h d) -> p h d", d=DK), back, inverse,
                                        ALU.mult).then_inc(att_ready, 1)
                nc.vector.tensor_tensor(back, back, inverse, ALU.mult).then_inc(att_ps_ready, 1)

            def add(j, g, half=1):
                cols = unit_cols(j, half)
                dve.wait_ge(att_ps_ready, unit(j, half) + 1)
                if g == 0:
                    if isinstance(j, int) and j == 0:
                        dve.wait_ge(first_loaded, 16)
                    else:
                        dve.wait_ge(first_rest_loaded, (T - 1) * 16)
                else:
                    dve.wait_ge(loaded[g], (j + 1) * 16)
                xs = x_slot(j, g, cols)
                a = att_ps[:, cols]
                nc.vector.tensor_tensor(xs, xs, a.unsqueeze(1).to_broadcast([P, BPG, a.shape[1]]),
                                        ALU.add).then_inc(added[g], 1)

            def heads(j, more, adds):
                adds = list(adds)
                for h in range(MAX_AHEAD, HEADS):
                    if adds and h % 2 == 0:
                        add(*adds.pop(0))
                    head_max(j, h)
                    if h % HPG == 2 and h > HPG:
                        invert_sums(j, h // HPG - 1)
                    if (h - AHEAD) % HPG == 0 and h > AHEAD:
                        copy_att_t(j, (h - AHEAD) // HPG - 1)
                    if h - AHEAD in laid_out_at(more):
                        g = (h - AHEAD + Q_SLOTS) // HPG
                        query_low(j + g // HG, g % HG)
                    if j == 0 and h == HALF_HEADS + FIRST_BACK + AHEAD - 1:
                        normalize(0, 0)
                        adds = [(0, g, 0) for g in DVE_GROUPS]
                while adds:
                    add(*adds.pop(0))
                invert_sums(j, HG - 1)
                if more:
                    for h in range(MAX_AHEAD):
                        head_max(j + 1, h)
                    query_low(j + 1, HALF_GROUPS - 1)
                copy_att_t(j, HG - 1)

            for what in steps:
                if what == "lay out queries":
                    for g in range(Q_SLOTS // HPG):
                        query_low(0, g)
                elif what == "first scores":
                    for h in range(MAX_AHEAD):
                        head_max(0, h)
                elif isinstance(what, int):
                    empty(what)
            heads(0, True, [])
            normalize(0)
            for j in range(1, T):
                heads(j, j + 1 < T, [(j - 1, g) for g in DVE_GROUPS])
                normalize(j)
            for g in DVE_GROUPS:
                add(T - 1, g)


_INS = ["x", "ctx_1024", "L0_xattn_Wq", "L0_xattn_Wk", "L0_xattn_Wv"]


def kernel(**inputs):
    import numpy as _np
    import concourse.bacc as _bacc
    from concourse import mybir as _mybir
    from concourse.bass_utils import run_bass_kernel_spmd as _run

    nc = _bacc.Bacc("TRN2", target_bir_lowering=False, num_devices=1)
    arrays, args = {}, []
    for name in _INS:
        a = _np.ascontiguousarray(inputs[name])
        arrays[f"in_{name}_dram"] = a
        args.append(nc.dram_tensor(f"in_{name}_dram", a.shape, _mybir.dt.from_np(a.dtype), kind="ExternalInput").ap())
    shape = arrays["in_x_dram"].shape
    out = nc.dram_tensor("out_0_dram", shape, _mybir.dt.float32, kind="ExternalOutput").ap()
    cross_attention_add(nc, *args, out)
    r = _run(nc, [arrays], core_ids=[0])
    return r.results[0]["out_0_dram"]
```
